# Optimizing a Trainium2 kernel written in Bass

```python
import numpy as np
import jax
import jax.numpy as jnp

def _softmax(x, axis=-1):
    return jax.nn.softmax(x, axis=axis)

def _gelu(x):
    return jax.nn.gelu(x, approximate=True)

def _silu(x):
    return jax.nn.silu(x)

def _sigmoid(x):
    return jax.nn.sigmoid(x)

def _layernorm(x, axis=-1, eps=1e-05):
    m = jnp.mean(x, axis=axis, keepdims=True)
    v = jnp.var(x, axis=axis, keepdims=True)
    return (x - m) / jnp.sqrt(v + eps)

def _scatter_add(tgt, idx, src, axis=0):
    return tgt.at[idx].add(src)

def _segment_sum(src, seg, n):
    return jax.ops.segment_sum(src, seg, n)
kernel_name = 'mk_conv_preact_d2_conv_nchw192_r2_73b36b'

def setup_inputs(seed: int=0):
    np.random.seed(seed)
    _w = jnp.asarray

    def _rec_inputs():
        import jax
        import jax.numpy as jnp
        _gk = jax.random.key(seed)
        x = -0.0001836 + 1 * jax.random.normal(jax.random.fold_in(_gk, 1), (4, 96, 128, 128), jnp.float32)
        return x
    x = _rec_inputs()

    def _L0_conv_setup():
        import jax, jax.numpy as jnp
        import numpy as np
        B, C, H, W = (8, 96, 128, 128)

        def _dwconv(x, w, pad):
            return jax.lax.conv_general_dilated(x, w, window_strides=(1, 1), padding=[(pad, pad), (pad, pad)], dimension_numbers=('NCHW', 'OIHW', 'NCHW'), feature_group_count=x.shape[1])
        key = jax.random.key(seed)
        k1, k2, k3, k4, k5 = jax.random.split(key, 5)
        x = jax.random.normal(k1, (B, C, H, W), dtype=jnp.float32)
        w1 = jax.random.normal(k2, (C, 1, 1, 1), dtype=jnp.float32) * 0.1
        w3 = jax.random.normal(k3, (C, 1, 3, 3), dtype=jnp.float32) * 0.1
        w5 = jax.random.normal(k4, (C, 1, 5, 5), dtype=jnp.float32) * 0.1
        alpha = jax.random.normal(k5, (4,), dtype=jnp.float32)
        return {'x': x, 'w1': w1, 'w3': w3, 'w5': w5, 'alpha': alpha}
    _L0_conv_all = _L0_conv_setup()
    _L0_conv_in = {k: v for k, v in _L0_conv_all.items() if k in ('w1', 'w3', 'w5', 'alpha')}
    del _L0_conv_all

    def _L1_conv_setup():
        import jax, jax.numpy as jnp
        import numpy as np
        from jax import lax
        key = jax.random.key(seed)
        k1, k2, k3 = jax.random.split(key, 3)
        B, C, H, W = (16, 96, 64, 64)
        x = jax.random.normal(k1, (B, C, H, W), dtype=jnp.float32)
        fan_in = 9.0
        bound = 1.0 / np.sqrt(fan_in)
        w = jax.random.uniform(k2, (1, 1, 3, 3), jnp.float32, -bound, bound)
        b = jax.random.uniform(k3, (1,), jnp.float32, -bound, bound)
        return {'x': x, 'w': w, 'b': b}
    _L1_conv_all = _L1_conv_setup()
    _L1_conv_in = {k: v for k, v in _L1_conv_all.items() if k in ('w', 'b')}
    del _L1_conv_all
    return {'x': x, 'L0_conv_w1': _L0_conv_in['w1'], 'L0_conv_w3': _L0_conv_in['w3'], 'L0_conv_w5': _L0_conv_in['w5'], 'L0_conv_alpha': _L0_conv_in['alpha'], 'L1_conv_w': _L1_conv_in['w'], 'L1_conv_b': _L1_conv_in['b']}

def reference(x, L0_conv_w1, L0_conv_w3, L0_conv_w5, L0_conv_alpha, L1_conv_w, L1_conv_b):
    import jax
    import jax.numpy as jnp

    def _L0_conv_ref(x, w1, w3, w5, alpha):
        import jax, jax.numpy as jnp
        import numpy as np
        B, C, H, W = (8, 96, 128, 128)

        def _dwconv(x, w, pad):
            return jax.lax.conv_general_dilated(x, w, window_strides=(1, 1), padding=[(pad, pad), (pad, pad)], dimension_numbers=('NCHW', 'OIHW', 'NCHW'), feature_group_count=x.shape[1])
        out1 = _dwconv(x, w1, 0)
        out3 = _dwconv(x, w3, 1)
        out5 = _dwconv(x, w5, 2)
        return alpha[0] * x + alpha[1] * out1 + alpha[2] * out3 + alpha[3] * out5

    def _L1_conv_ref(x, w, b):
        import jax, jax.numpy as jnp
        import numpy as np
        from jax import lax
        B, C, H, W = x.shape
        xr = x.reshape(B * C, 1, H, W)
        y = lax.conv_general_dilated(xr, w, window_strides=(1, 1), padding=((1, 1), (1, 1)), dimension_numbers=('NCHW', 'OIHW', 'NCHW'))
        y = y + b[None, :, None, None]
        return y.reshape(B, C, H, W)

    def _gn(v, G=32, eps=1e-05):
        B_, C_, H_, W_ = v.shape
        g = v.reshape(B_, G, C_ // G, H_, W_)
        m = jnp.mean(g, axis=(2, 3, 4), keepdims=True)
        s = jnp.var(g, axis=(2, 3, 4), keepdims=True)
        return ((g - m) / jnp.sqrt(s + eps)).reshape(v.shape)

    def _ln_c(v, eps=1e-06):
        m = jnp.mean(v, axis=1, keepdims=True)
        s = jnp.var(v, axis=1, keepdims=True)
        return (v - m) / jnp.sqrt(s + eps)

    def _ln_t(v, eps=1e-05):
        m = jnp.mean(v, axis=-1, keepdims=True)
        s = jnp.var(v, axis=-1, keepdims=True)
        return (v - m) / jnp.sqrt(s + eps)

    def _to_tokens(v):
        B_, C_, H_, W_ = v.shape
        return v.reshape(B_, C_, H_ * W_).transpose(0, 2, 1)

    def _from_tokens(t, like):
        B_, C_, H_, W_ = like.shape
        return t.transpose(0, 2, 1).reshape(B_, C_, H_, W_)
    x = x + _L0_conv_ref(_gn(x), L0_conv_w1, L0_conv_w3, L0_conv_w5, L0_conv_alpha)
    x = x + _L1_conv_ref(_gn(x), L1_conv_w, L1_conv_b)
    return x

_drawn_inputs = setup_inputs


def setup_inputs(seed=0):
    import zlib

    import numpy as np

    out = dict(_drawn_inputs(seed))
    spreads = {}
    factors = {}
    for name, (base, spread) in spreads.items():
        noise = np.random.default_rng([zlib.crc32(name.encode()), seed]).standard_normal(out[name].shape)
        drawn = base * np.exp(spread * noise) if base else spread * noise
        out[name] = jnp.asarray(drawn.astype(out[name].dtype))
    for name, factor in factors.items():
        out[name] = (out[name] * factor).astype(out[name].dtype)
    return out
```

```python
import concourse.bass as bass
from concourse import mybir
from contextlib import ExitStack



def preact_conv_stack(nc: bass.Bass, x: bass.AP, w1: bass.AP, w3: bass.AP, w5: bass.AP, alpha: bass.AP,
                      w_b: bass.AP, b_b: bass.AP, out: bass.AP):
    fp32 = mybir.dt.float32
    fp16 = mybir.dt.float16
    i32 = mybir.dt.int32
    ALU = mybir.AluOpType
    ACT = mybir.ActivationFunctionType
    AX = mybir.AxisListType

    NB, C, H, W = x.shape
    GROUPS = 32
    CG = C // GROUPS
    NU = GROUPS
    CH = NB * W
    K5 = 5
    PAD = K5 // 2
    WP = W + 2 * PAD
    NM = 2 * K5
    TOEP = 2 * H - 1
    NK = C + 1
    GN_EPS = 1e-5
    HALF = CG * W // 2
    G_SCALE = 256.0
    W_SCALE = 2.0 ** 14

    ctx = ExitStack()
    with ctx:
        def sb(name, shape, dt=fp32):
            return ctx.enter_context(nc.sbuf_tensor(name, shape, dt))

        def sem(name):
            return ctx.enter_context(nc.semaphore(name))

        diag_dram = nc.dram_tensor("diag_scratch", [NK, TOEP * NM], fp16, kind="Internal").ap()
        unscale_dram = nc.dram_tensor("unscale_scratch", [NK, 1], fp32, kind="Internal").ap()

        k_w1 = sb("k_w1", [NK, 1])
        k_w3 = sb("k_w3", [NK, 3, 3])
        k_w5 = sb("k_w5", [NK, K5, K5])
        k_alpha = sb("k_alpha", [NK, 4])
        kern = sb("kern", [NK, K5, K5])
        k_mid = sb("k_mid", [NK, 1])
        k_max = sb("k_max", [NK, 1])
        k_min = sb("k_min", [NK, 1])
        k_pow = sb("k_pow", [NK, 1])
        k_inv = sb("k_inv", [NK, 1])
        k_unscale = sb("k_unscale", [NK, 1])
        diag = sb("diag", [NK, TOEP, NM], fp16)

        unscale = sb("unscale", [H, NK])
        bias_b = sb("bias_b", [H, 1])
        ones_mean = sb("ones_mean", [H, H])
        ones_var = sb("ones_var", [H, H])
        eps_t = sb("eps_t", [H, 1])
        band3 = sb("band3", [H, H * NM], fp16)

        xt = sb("xt", [H, 2, NB, CG, W])
        band3_raw = sb("band3_raw", [H, H * NM], fp16)
        band_raw = sb("band_raw", [H, 2, CG, H * NM], fp16)
        band5 = sb("band5", [H, 2, CG, H * NM], fp16)
        x1 = sb("x1", [H, 2, NB, CG, W])
        gn_f = [sb(f"gn_f{s}", [H, NB, CG, W]) for s in "XY"]
        gn_hi = [sb(f"gn_hi{s}", [H, 2, NB, CG, WP], fp16) for s in "XY"]
        gn_lo = [sb(f"gn_lo{s}", [H, 2, NB, CG, WP], fp16) for s in "XY"]
        conv_b = sb("conv_b", [H, 2, CG, CH])
        out_t = sb("out_t", [H, 2, CG, CH])

        stats = [sb(f"stats{s}", [H, NB, 6]) for s in "XY"]
        mean = [sb(f"mean{s}", [H, NB]) for s in "XY"]
        dev = [sb(f"dev{s}", [H, NB, 2]) for s in "XY"]
        var = [sb(f"var{s}", [H, NB]) for s in "XY"]
        std = [sb(f"std{s}", [H, NB]) for s in "XY"]
        r0 = [sb(f"r0{s}", [H, NB]) for s in "XY"]
        nt = [sb(f"nt{s}", [H, 3, NB]) for s in "XY"]
        g_mul = [sb(f"g_mul{s}", [H, NB]) for s in "XY"]
        g_add = [sb(f"g_add{s}", [H, NB]) for s in "XY"]

        ps1 = ctx.enter_context(nc.psum_tensor("ps1", [H, CG, CH], fp32))
        ps2 = ctx.enter_context(nc.psum_tensor("ps2", [H, CG, CH], fp32))
        ps_s = [ctx.enter_context(nc.psum_tensor(f"ps_s{s}", [H, 512], fp32)) for s in "XY"]

        k_in = sem("k_in")
        k_zero = sem("k_zero")
        diag_zero = sem("diag_zero")
        k_step = sem("k_step")
        k_out = sem("k_out")
        c_in = sem("c_in")
        const_ready = sem("const_ready")
        pads_zero = sem("pads_zero")
        flipped = sem("flipped")
        flip3_done = sem("flip3_done")
        x_in = [sem(f"x_in{p}") for p in range(2)]
        band_in = [sem(f"band_in{p}") for p in range(2)]
        stored = [sem(f"stored{p}") for p in range(2)]
        conv_done = [sem("conv1_done"), sem("conv2_done")]
        evac1_done = sem("evac1_done")
        stats_done = [sem(f"stats_done{s}") for s in "XY"]
        mean_done = [sem(f"mean_done{s}") for s in "XY"]
        dev_done = [sem(f"dev_done{s}") for s in "XY"]
        var_done = [sem(f"var_done{s}") for s in "XY"]
        var_read = [sem(f"var_read{s}") for s in "XY"]
        std_done = [sem(f"std_done{s}") for s in "XY"]
        norm_step = [sem(f"norm_step{s}") for s in "XY"]
        g_mul_done = [sem(f"g_mul_done{s}") for s in "XY"]
        affine_ready = [sem(f"affine_ready{s}") for s in "XY"]
        gn_done = [sem(f"gn_done{s}") for s in "XY"]
        hi_done = [sem(f"hi_done{s}") for s in "XY"]
        lo_done = [sem(f"lo_done{s}") for s in "XY"]
        conv_b_done = sem("conv_b_done")
        out_done = sem("out_done")
        X, Y = 0, 1
        STEPS = 7

        block = ctx.enter_context(nc.Block())

        def over_slots(eng, slot):
            slot(0, 0)
            slot(1, 1)
            slot(2, 0)
            with eng.Fori(3, NU - 1, 2) as k:
                slot(k, 1)
                slot(k + 1, 0)
            slot(NU - 1, 1)
            slot(NU, 0)

        def first(k):
            return isinstance(k, int) and k == 0

        def last(k):
            return isinstance(k, int) and k == NU

        def early(k):
            return isinstance(k, int) and k < 2

        @block.sync
        def _(sp):
            sp.wait_ge(k_zero, 5)
            with nc.allow_non_contiguous_dma(reason="a few small weights"):
                sp.dma_start(k_w1[0:C, :], w1.rearrange("c a h w -> c (a h w)")).then_inc(k_in, 16)
                sp.dma_start(k_w3[0:C, :, :], w3.rearrange("c a h w -> c (a h) w")).then_inc(k_in, 16)
                sp.dma_start(k_w5[0:C, :, :], w5.rearrange("c a h w -> c (a h) w")).then_inc(k_in, 16)
                sp.dma_start(k_alpha[0:C, :], alpha.rearrange("(a n) -> a n", a=1).to_broadcast([C, 4])).then_inc(k_in, 16)
                sp.dma_start(k_w3[C:NK, :, :], w_b.rearrange("c a h w -> c (a h) w")).then_inc(k_in, 16)
                sp.dma_start(bias_b[:, :], b_b.rearrange("(a n) -> a n", a=1).to_broadcast([H, 1])).then_inc(c_in, 16)

            def load_x(k, p, c):
                sp.dma_start(xt[:, p, :, c, :], x[:, bass.ds(CG * k + c, 1), :, :].rearrange("b c h w -> h (b c) w"))\
                  .then_inc(x_in[p], 16)

            def load_band(k, p, c):
                row = diag_dram[bass.ds(CG * k + c, 1), :]
                sp.dma_start(band_raw[:, p, c, :], bass.AP(row.tensor, row.offset, [[NM, H], [1, H * NM]]))\
                  .then_inc(band_in[p], 16)

            for k in range(2):
                for c in range(CG):
                    load_x(k, k, c)
            sp.wait_ge(k_step, 12)
            sp.dma_start(diag_dram[:, :], diag[:, :, :].rearrange("k d m -> k (d m)")).then_inc(k_out, 16)
            sp.dma_start(unscale_dram[:, :], k_unscale[:, :]).then_inc(k_out, 16)
            sp.wait_ge(k_out, 32)
            for c in range(CG):
                load_band(0, 0, c)
            with nc.allow_non_contiguous_dma(reason="one value for each partition and kernel"):
                sp.dma_start(unscale[:, :], unscale_dram.rearrange("k a -> a k").to_broadcast([H, NK])).then_inc(c_in, 16)
            shared = diag_dram[C:NK, :]
            sp.dma_start(band3_raw[:, :], bass.AP(shared.tensor, shared.offset, [[NM, H], [1, H * NM]])).then_inc(c_in, 16)
            for c in range(CG):
                load_band(1, 1, c)

            def slot(k, p, loads=True):
                if not first(k):
                    for c in range(CG):
                        sp.wait_ge(out_done, CG * (k - 1) + c + 1)
                        sp.dma_start(out[:, bass.ds(CG * (k - 1) + c, 1), :, :].rearrange("b c h w -> h (b c) w"),
                                     out_t[:, 1 - p, c, :].rearrange("h (b w) -> h b w", b=NB))\
                          .then_inc(stored[1 - p], 16)

            def fetch(k, p):
                for c in range(CG):
                    sp.wait_ge(evac1_done, CG * k + c + 1)
                    load_x(k + 2, p, c)
                for c in range(CG):
                    sp.wait_ge(flipped, CG * k + c + 1)
                    load_band(k + 2, p, c)

            fetch(0, 0)
            with sp.Fori(1, NU - 3, 2) as k:
                fetch(k, 1)
                slot(k, 1)
                fetch(k + 1, 0)
                slot(k + 1, 0)
            fetch(NU - 3, 1)
            slot(NU - 3, 1)
            slot(NU - 2, 0)
            slot(NU - 1, 1)
            slot(NU, 0)
            for p in range(2):
                sp.wait_ge(stored[p], 16 * CG * NU // 2)

        @block.tensor
        def _(pe):
            def conv(which, k, p, c, taps):
                src_hi, src_lo, dst = gn_hi[which], gn_lo[which], (ps1, ps2)[which]
                band = band5[:, p, c, :] if which == X else band3[:, :]
                parts = [(t, m, src) for t in taps for m, src in ((t, src_hi), (t, src_lo), (K5 + t, src_hi))]
                for n, (t, m, src) in enumerate(parts):
                    mm = nc.tensor.matmul(dst[:, c, :], band[:, m::NM], src[:, p, :, c, t:t + W],
                                          start=(n == 0), stop=(n == len(parts) - 1))
                mm.then_inc(conv_done[which], 1)

            def mean_product(s, n):
                pe.wait_ge(stats_done[s], n + 1)
                nc.tensor.matmul(ps_s[s][:, 0:2 * NB], ones_mean[:, :],
                                 stats[s][:, :, :].rearrange("h b (e s) -> h b e s", e=2)[:, :, :, 1],
                                 start=True, stop=True).then_inc(mean_done[s], 1)

            def var_product(s, n):
                pe.wait_ge(dev_done[s], n + 1)
                nc.tensor.matmul(ps_s[s][:, 0:6 * NB], ones_var[:, :], stats[s][:, :, :].rearrange("h b s -> h (b s)"),
                                 start=True, stop=True).then_inc(var_done[s], 1)

            pe.wait_ge(const_ready, 3)
            pe.wait_ge(pads_zero, 8)
            mean_product(X, 0)
            var_product(X, 0)
            pe.wait_ge(flip3_done, 1)

            def slot(k, p):
                if not last(k):
                    pe.wait_ge(hi_done[X], NB * (k + 1))
                    pe.wait_ge(lo_done[X], k + 1)
                    for c in range(CG):
                        pe.wait_ge(flipped, CG * k + c + 1)
                        if not first(k):
                            pe.wait_ge(evac1_done, CG * (k - 1) + c + 1)
                        conv(X, k, p, c, range(K5))
                        if not (isinstance(k, int) and k == NU - 1):
                            if c == 0:
                                pe.wait_ge(var_read[X], k + 1)
                                mean_product(X, k + 1)
                            elif c == 1:
                                var_product(X, k + 1)
                for c in range(CG):
                    if not first(k):
                        if c == 0:
                            pe.wait_ge(hi_done[Y], NB * k)
                            pe.wait_ge(lo_done[Y], k)
                        if not early(k):
                            pe.wait_ge(conv_b_done, CG * (k - 2) + c + 1)
                        conv(Y, k - 1, 1 - p, c, range(1, K5 - 1))
                    if not last(k):
                        if c == 1:
                            if not first(k):
                                pe.wait_ge(var_read[Y], k)
                            mean_product(Y, k)
                        elif c == 2:
                            var_product(Y, k)

            over_slots(pe, slot)

        @block.scalar
        def _(act):
            act.wait_ge(const_ready, 3)

            def root(s, n):
                act.wait_ge(norm_step[s], STEPS * n + 3)
                nc.scalar.activation(std[s][:, :], var[s][:, :], ACT.Sqrt, bias=eps_t[:, 0:1]).then_inc(std_done[s], 1)

            def normalize(s, n, p, src):
                act.wait_ge(affine_ready[s], n + 1)
                if not first(n):
                    act.wait_ge(lo_done[s], n)
                if not early(n):
                    act.wait_ge(conv_done[s], CG * (n - 1))
                for b in range(NB):
                    nc.scalar.activation(gn_f[s][:, b, :, :], src[:, p, b, :, :], ACT.Identity,
                                         bias=g_add[s][:, b:b + 1], scale=g_mul[s][:, b:b + 1]).then_inc(gn_done[s], 1)
                    nc.scalar.activation(gn_hi[s][:, p, b, :, PAD:PAD + W], src[:, p, b, :, :], ACT.Identity,
                                         bias=g_add[s][:, b:b + 1], scale=g_mul[s][:, b:b + 1]).then_inc(hi_done[s], 1)

            root(X, 0)
            normalize(X, 0, 0, xt)
            act.wait_ge(c_in, 48)

            def slot(k, p):
                if not first(k):
                    root(Y, k - 1)
                    normalize(Y, k - 1, 1 - p, x1)
                if not last(k) and not (isinstance(k, int) and k == NU - 1):
                    root(X, k + 1)
                    normalize(X, k + 1, 1 - p, xt)
                if not first(k):
                    for c in range(CG):
                        act.wait_ge(conv_done[Y], CG * (k - 1) + c + 1)
                        if not early(k) and not (isinstance(k, int) and k < 3):
                            act.wait_ge(out_done, CG * (k - 3) + c + 1)
                        nc.scalar.activation(conv_b[:, 1 - p, c, :], ps2[:, c, :], ACT.Identity, bias=bias_b[:, 0:1],
                                             scale=unscale[:, C:NK]).then_inc(conv_b_done, 1)

            over_slots(act, slot)

        @block.vector
        def _(dve):
            for t in (k_w1[:, :], k_w3[:, :, :], k_w5[:, :, :], k_alpha[:, :]):
                nc.vector.memset(t, 0.0).then_inc(k_zero, 1)
            dve.wait_ge(k_zero, 4)
            nc.vector.memset(k_alpha[C:NK, 2:3], 1.0).then_inc(k_zero, 1)
            nc.vector.memset(ones_mean[:, :], 1.0 / (2 * H)).then_inc(const_ready, 1)
            nc.vector.memset(ones_var[:, :], 1.0 / (2 * H * HALF)).then_inc(const_ready, 1)
            nc.vector.memset(eps_t[:, :], GN_EPS).then_inc(const_ready, 1)
            for s in (X, Y):
                for part in (gn_hi, gn_lo):
                    for at in (0, PAD + W):
                        nc.vector.memset(part[s][:, :, :, :, at:at + PAD].rearrange("h p b c w -> h (p b c) w"), 0.0)\
                          .then_inc(pads_zero, 1)

            dve.wait_ge(k_in, 80)
            nc.vector.tensor_scalar(kern[:, :, :], k_w5[:, :, :], k_alpha[:, 3:4], None, ALU.mult).then_inc(k_step, 1)
            nc.vector.scalar_tensor_tensor(out=k_mid[:, :], in0=k_w1[:, :], scalar=k_alpha[:, 1:2], in1=k_alpha[:, 0:1],
                                           op0=ALU.mult, op1=ALU.add).then_inc(k_step, 1)
            dve.wait_ge(k_step, 2)
            nc.vector.scalar_tensor_tensor(out=kern[:, 1:4, 1:4], in0=k_w3[:, :, :], scalar=k_alpha[:, 2:3],
                                           in1=kern[:, 1:4, 1:4], op0=ALU.mult, op1=ALU.add).then_inc(k_step, 1)
            dve.wait_ge(k_step, 3)
            nc.vector.tensor_tensor(kern[:, 2, 2:3], kern[:, 2, 2:3], k_mid[:, :], ALU.add).then_inc(k_step, 1)
            dve.wait_ge(k_step, 4)
            nc.vector.tensor_reduce(k_max[:, :], kern[:, :, :], AX.XY, ALU.max)
            nc.vector.tensor_reduce(k_min[:, :], kern[:, :, :], AX.XY, ALU.min).then_inc(k_step, 1)
            dve.wait_ge(k_step, 5)
            nc.vector.scalar_tensor_tensor(out=k_pow[:, :], in0=k_min[:, :], scalar=-1.0, in1=k_max[:, :],
                                           op0=ALU.mult, op1=ALU.max).then_inc(k_step, 1)
            dve.wait_ge(k_step, 6)
            nc.vector.tensor_scalar(k_pow[:, :], k_pow[:, :], 2.0 ** -100, None, ALU.max).then_inc(k_step, 1)
            dve.wait_ge(k_step, 7)
            nc.vector.tensor_scalar(k_pow[:, :].bitcast(i32), k_pow[:, :].bitcast(i32), 0x7F800000, None,
                                    ALU.bitwise_and).then_inc(k_step, 1)
            dve.wait_ge(k_step, 8)
            nc.vector.reciprocal(k_inv[:, :], k_pow[:, :])
            nc.vector.tensor_scalar(k_unscale[:, :], k_pow[:, :], 1.0 / (W_SCALE * G_SCALE), None, ALU.mult)\
              .then_inc(k_step, 1)
            dve.wait_ge(k_step, 9)
            nc.vector.tensor_scalar(kern[:, :, :], kern[:, :, :], k_inv[:, 0:1], W_SCALE, ALU.mult, ALU.mult)\
              .then_inc(k_step, 1)
            dve.wait_ge(k_step, 10)
            dve.wait_ge(diag_zero, 1)
            mid = diag[:, H - 1 - PAD:H + PAD, :]
            nc.vector.tensor_copy(mid[:, :, 0:K5], kern[:, :, :]).then_inc(k_step, 1)
            dve.wait_ge(k_step, 11)
            nc.vector.tensor_tensor(mid[:, :, K5:NM], kern[:, :, :], mid[:, :, 0:K5], ALU.subtract).then_inc(k_step, 1)

            def row_stats(s, n, p, src):
                if s == X:
                    dve.wait_ge(x_in[p], 16 * CG * ((n - p) // 2 + 1) if isinstance(n, int) else 8 * CG * (n - p) + 16 * CG)
                else:
                    dve.wait_ge(evac1_done, CG * (n + 1))
                if not first(n):
                    dve.wait_ge(var_done[s], n)
                for b in range(NB):
                    st = nc.vector.bn_stats(stats[s][:, b, :], src[:, p, b, :, :].rearrange("h c w -> h (c w)"))
                st.then_inc(stats_done[s], 1)

            def deviations(s, n):
                halves = stats[s][:, :, :].rearrange("h b (e s) -> h b e s", e=2)[:, :, :, 1]
                dve.wait_ge(mean_done[s], n + 1)
                nc.vector.tensor_reduce(mean[s][:, :], ps_s[s][:, 0:2 * NB].rearrange("h (b e) -> h b e", e=2),
                                        AX.X, ALU.add).then_inc(norm_step[s], 1)
                dve.wait_ge(norm_step[s], STEPS * n + 1)
                nc.vector.tensor_tensor(dev[s][:, :, :], halves, mean[s][:, :].unsqueeze(2).to_broadcast([H, NB, 2]),
                                        ALU.subtract).then_inc(norm_step[s], 1)
                dve.wait_ge(norm_step[s], STEPS * n + 2)
                nc.vector.scalar_tensor_tensor(out=halves, in0=dev[s][:, :, :], scalar=float(HALF), in1=dev[s][:, :, :],
                                               op0=ALU.mult, op1=ALU.mult).then_inc(dev_done[s], 1)

            def variance(s, n):
                dve.wait_ge(var_done[s], n + 1)
                sums = ps_s[s][:, 0:6 * NB].rearrange("h (b e s) -> h b e s", e=2, s=3)[:, :, :, 1:3]
                nc.vector.tensor_reduce(var[s][:, :], sums, AX.XY, ALU.add).then_inc(norm_step[s], 1)
                dve.wait_ge(norm_step[s], STEPS * n + 3)
                nc.vector.tensor_scalar(nt[s][:, 0, :], var[s][:, :], GN_EPS, None, ALU.add).then_inc(var_read[s], 1)

            def affine(s, n):
                dve.wait_ge(std_done[s], n + 1)
                nc.vector.reciprocal(r0[s][:, :], std[s][:, :]).then_inc(norm_step[s], 1)
                dve.wait_ge(norm_step[s], STEPS * n + 4)
                nc.vector.tensor_tensor(nt[s][:, 1, :], r0[s][:, :], r0[s][:, :], ALU.mult).then_inc(norm_step[s], 1)
                dve.wait_ge(norm_step[s], STEPS * n + 5)
                nc.vector.tensor_tensor(nt[s][:, 2, :], nt[s][:, 1, :], nt[s][:, 0, :], ALU.mult).then_inc(norm_step[s], 1)
                dve.wait_ge(norm_step[s], STEPS * n + 6)
                nc.vector.tensor_scalar(nt[s][:, 2, :], nt[s][:, 2, :], -0.5 * G_SCALE, 1.5 * G_SCALE,
                                        ALU.mult, ALU.add).then_inc(norm_step[s], 1)
                dve.wait_ge(norm_step[s], STEPS * n + 7)
                if not first(n):
                    dve.wait_ge(hi_done[s], NB * n)
                nc.vector.tensor_tensor(g_mul[s][:, :], nt[s][:, 2, :], r0[s][:, :], ALU.mult).then_inc(g_mul_done[s], 1)
                dve.wait_ge(g_mul_done[s], n + 1)
                nc.vector.scalar_tensor_tensor(out=g_add[s][:, :], in0=mean[s][:, :], scalar=-1.0, in1=g_mul[s][:, :],
                                               op0=ALU.mult, op1=ALU.mult).then_inc(affine_ready[s], 1)

            def low_part(s, n, p):
                dve.wait_ge(hi_done[s], NB * (n + 1))
                if not early(n):
                    dve.wait_ge(conv_done[s], CG * (n - 1))
                nc.vector.tensor_tensor(gn_lo[s][:, p, :, :, PAD:PAD + W].rearrange("h b c w -> h (b c) w"),
                                        gn_f[s][:, :, :, :].rearrange("h b c w -> h (b c) w"),
                                        gn_hi[s][:, p, :, :, PAD:PAD + W].rearrange("h b c w -> h (b c) w"),
                                        ALU.subtract).then_inc(lo_done[s], 1)

            def evacuate(k, p, c):
                dve.wait_ge(conv_done[X], CG * k + c + 1)
                if not early(k):
                    dve.wait_ge(out_done, CG * (k - 2) + c + 1)
                nc.vector.scalar_tensor_tensor(
                    out=x1[:, p, :, c, :], in0=ps1[:, c, :].rearrange("h (b w) -> h b w", b=NB),
                    scalar=unscale[:, bass.ds(CG * k + c, 1)], in1=xt[:, p, :, c, :],
                    op0=ALU.mult, op1=ALU.add).then_inc(evac1_done, 1)

            def in_order(dst, src):
                return nc.vector.tensor_copy(dst.bitcast(i32).rearrange("h (o m) -> h o m", m=NM // 2),
                                             src.bitcast(i32).rearrange("h (o m) -> h o m", m=NM // 2)[:, ::-1, :])

            def in_order_unit(k, p):
                dve.wait_ge(band_in[p], 16 * CG * ((k - p) // 2 + 1) if isinstance(k, int) else 8 * CG * (k - p) + 16 * CG)
                for c in range(CG):
                    if not early(k):
                        dve.wait_ge(conv_done[X], CG * (k - 2) + c + 1)
                    in_order(band5[:, p, c, :], band_raw[:, p, c, :]).then_inc(flipped, 1)

            row_stats(X, 0, 0, xt)
            deviations(X, 0)
            variance(X, 0)
            affine(X, 0)
            low_part(X, 0, 0)
            in_order_unit(0, 0)
            row_stats(X, 1, 1, xt)
            dve.wait_ge(c_in, 48)
            in_order(band3[:, :], band3_raw[:, :]).then_inc(flip3_done, 1)

            def slot(k, p):
                ahead = not last(k) and not (isinstance(k, int) and k == NU - 1)
                if not first(k):
                    variance(Y, k - 1)
                    affine(Y, k - 1)
                if not last(k):
                    evacuate(k, p, 0)
                if ahead:
                    deviations(X, k + 1)
                if not first(k):
                    low_part(Y, k - 1, 1 - p)
                if not last(k):
                    evacuate(k, p, 1)
                if ahead:
                    variance(X, k + 1)
                    affine(X, k + 1)
                if not last(k):
                    evacuate(k, p, 2)
                    row_stats(Y, k, p, x1)
                if ahead:
                    in_order_unit(k + 1, 1 - p)
                    low_part(X, k + 1, 1 - p)
                if not last(k):
                    deviations(Y, k)
                if ahead and not (isinstance(k, int) and k == NU - 2):
                    row_stats(X, k + 2, p, xt)

            slot(0, 0)
            slot(1, 1)
            slot(2, 0)
            with dve.Fori(3, NU - 3, 2) as k:
                slot(k, 1)
                slot(k + 1, 0)
            slot(NU - 3, 1)
            slot(NU - 2, 0)
            slot(NU - 1, 1)
            slot(NU, 0)

        @block.gpsimd
        def _(pool):
            nc.gpsimd.memset(diag[:, :, :], 0.0).then_inc(diag_zero, 1)

            def residual_sum(k, p):
                for c in range(CG):
                    pool.wait_ge(conv_b_done, CG * k + c + 1)
                    if c == 0 and not early(k):
                        pool.wait_ge(stored[p], 16 * CG * ((k - p) // 2) if isinstance(k, int) else 8 * CG * (k - p))
                    nc.gpsimd.tensor_tensor(out_t[:, p, c, :].rearrange("h (b w) -> h b w", b=NB), x1[:, p, :, c, :],
                                            conv_b[:, p, c, :].rearrange("h (b w) -> h b w", b=NB),
                                            ALU.add).then_inc(out_done, 1)

            residual_sum(0, 0)
            residual_sum(1, 1)
            with pool.Fori(2, NU, 2) as k:
                residual_sum(k, 0)
                residual_sum(k + 1, 1)


_INS = ["x", "L0_conv_w1", "L0_conv_w3", "L0_conv_w5", "L0_conv_alpha", "L1_conv_w", "L1_conv_b"]


def kernel(**inputs):
    import numpy as _np
    import concourse.bacc as _bacc
    from concourse import mybir as _mybir
    from concourse.bass_utils import run_bass_kernel_spmd as _run

    nc = _bacc.Bacc("TRN2", target_bir_lowering=False, num_devices=1)
    arrays, args = {}, []
    for name in _INS:
        a = _np.ascontiguousarray(inputs[name])
        arrays[f"in_{name}_dram"] = a
        args.append(nc.dram_tensor(f"in_{name}_dram", a.shape, _mybir.dt.from_np(a.dtype), kind="ExternalInput").ap())
    args.append(nc.dram_tensor("out_0_dram", inputs["x"].shape, _mybir.dt.float32, kind="ExternalOutput").ap())
    preact_conv_stack(nc, *args)
    r = _run(nc, [arrays], core_ids=[0])
    return r.results[0]["out_0_dram"]
```

```python
import concourse.bass as bass
from concourse import mybir
from contextlib import ExitStack



def preact_conv_stack(nc: bass.Bass, x: bass.AP, w1: bass.AP, w3: bass.AP, w5: bass.AP, alpha: bass.AP,
                      w_b: bass.AP, b_b: bass.AP, out: bass.AP):
    fp32 = mybir.dt.float32
    fp16 = mybir.dt.float16
    i32 = mybir.dt.int32
    ALU = mybir.AluOpType
    ACT = mybir.ActivationFunctionType
    AX = mybir.AxisListType

    NB, C, H, W = x.shape
    GROUPS = 32
    CG = C // GROUPS
    NU = GROUPS
    CH = NB * W
    NX = 4
    K5 = 5
    PAD = K5 // 2
    WP = W + 2 * PAD
    NM = 2 * K5
    TOEP = 2 * H - 1
    NK = C + 1
    GN_EPS = 1e-5
    HALF = CG * W // 2
    G_SCALE = 256.0
    W_SCALE = 2.0 ** 14

    ctx = ExitStack()
    with ctx:
        def sb(name, shape, dt=fp32):
            return ctx.enter_context(nc.sbuf_tensor(name, shape, dt))

        def sem(name):
            return ctx.enter_context(nc.semaphore(name))

        diag_dram = nc.dram_tensor("diag_scratch", [NK, TOEP * NM], fp16, kind="Internal").ap()
        unscale_dram = nc.dram_tensor("unscale_scratch", [NK, 1], fp32, kind="Internal").ap()

        k_w1 = sb("k_w1", [NK, 1])
        k_w3 = sb("k_w3", [NK, 3, 3])
        k_w5 = sb("k_w5", [NK, K5, K5])
        k_alpha = sb("k_alpha", [NK, 4])
        kern = sb("kern", [NK, K5, K5])
        k_mid = sb("k_mid", [NK, 1])
        k_max = sb("k_max", [NK, 1])
        k_min = sb("k_min", [NK, 1])
        k_pow = sb("k_pow", [NK, 1])
        k_inv = sb("k_inv", [NK, 1])
        k_unscale = sb("k_unscale", [NK, 1])
        diag = sb("diag", [NK, TOEP, NM], fp16)

        unscale = sb("unscale", [H, NK])
        bias_b = sb("bias_b", [H, 1])
        ones_mean = sb("ones_mean", [H, H])
        ones_var = sb("ones_var", [H, H])
        eps_t = sb("eps_t", [H, 1])
        band3 = sb("band3", [H, H * NM], fp16)

        xt = sb("xt", [H, NX, NB, CG, W])
        band3_raw = sb("band3_raw", [H, H * NM], fp16)
        band_raw = sb("band_raw", [H, 2, CG, H * NM], fp16)
        band5 = sb("band5", [H, 2, CG, H * NM], fp16)
        x1 = sb("x1", [H, 2, NB, CG, W])
        gn_f = [sb(f"gn_f{s}", [H, NB, CG, W]) for s in "XY"]
        gn_hi = [sb(f"gn_hi{s}", [H, 2, NB, CG, WP], fp16) for s in "XY"]
        gn_lo = [sb(f"gn_lo{s}", [H, 2, NB, CG, WP], fp16) for s in "XY"]
        conv_b = sb("conv_b", [H, 2, CG, CH])
        out_t = sb("out_t", [H, 2, CG, CH])

        stats = sb("stats", [H, 2, NB, 6])
        mean = sb("mean", [H, 2 * NB])
        dev = sb("dev", [H, 2 * NB, 2])
        var = sb("var", [H, 2 * NB])
        var_eps = sb("var_eps", [H, 2 * NB])
        std = sb("std", [H, 2 * NB])
        r0 = sb("r0", [H, 2 * NB])
        newton = sb("newton", [H, 2 * NB])
        g_mul = sb("g_mul", [H, 2 * NB])
        g_add = sb("g_add", [H, 2 * NB])

        ps1 = ctx.enter_context(nc.psum_tensor("ps1", [H, CG, CH], fp32))
        ps2 = ctx.enter_context(nc.psum_tensor("ps2", [H, CG, CH], fp32))
        ps_s = ctx.enter_context(nc.psum_tensor("ps_s", [H, CH], fp32))

        k_in = sem("k_in")
        k_zero = sem("k_zero")
        diag_zero = sem("diag_zero")
        k_step = sem("k_step")
        k_out = sem("k_out")
        c_in = sem("c_in")
        const_ready = sem("const_ready")
        pads_zero = sem("pads_zero")
        flipped = sem("flipped")
        flip3_done = sem("flip3_done")
        x_in = [sem(f"x_in{r}") for r in range(NX)]
        band_in = [sem(f"band_in{p}") for p in range(2)]
        stored = [sem(f"stored{p}") for p in range(2)]
        conv_done = [sem("conv1_done"), sem("conv2_done")]
        evac1_done = sem("evac1_done")
        stats_done = sem("stats_done")
        mean_done = sem("mean_done")
        dev_done = sem("dev_done")
        var_done = sem("var_done")
        var_read = sem("var_read")
        std_done = sem("std_done")
        norm_step = sem("norm_step")
        affine_ready = sem("affine_ready")
        gn_done = [sem(f"gn_done{s}") for s in "XY"]
        hi_done = [sem(f"hi_done{s}") for s in "XY"]
        lo_done = [sem(f"lo_done{s}") for s in "XY"]
        conv_b_done = sem("conv_b_done")
        out_done = sem("out_done")
        X, Y = 0, 1
        NORM_OPS = 8

        block = ctx.enter_context(nc.Block())

        PEEL = 3

        def over_slots(eng, slot, end):
            for k in range(PEEL):
                slot(k, k % NX)
            with eng.Fori(PEEL, end - NX + 1, NX) as k:
                for j in range(NX):
                    slot(k + j, (PEEL + j) % NX)
            for k in range(end, NU + 1):
                slot(k, k % NX)

        def static(k):
            return isinstance(k, int)

        def landed(n, buffers, r):
            return 16 * CG // buffers * (n - r) + 16 * CG

        @block.sync
        def _(sp):
            sp.wait_ge(k_zero, 5)
            with nc.allow_non_contiguous_dma(reason="a few small weights"):
                sp.dma_start(k_w1[0:C, :], w1.rearrange("c a h w -> c (a h w)")).then_inc(k_in, 16)
                sp.dma_start(k_w3[0:C, :, :], w3.rearrange("c a h w -> c (a h) w")).then_inc(k_in, 16)
                sp.dma_start(k_w5[0:C, :, :], w5.rearrange("c a h w -> c (a h) w")).then_inc(k_in, 16)
                sp.dma_start(k_alpha[0:C, :], alpha.rearrange("(a n) -> a n", a=1).to_broadcast([C, 4])).then_inc(k_in, 16)
                sp.dma_start(k_w3[C:NK, :, :], w_b.rearrange("c a h w -> c (a h) w")).then_inc(k_in, 16)
                sp.dma_start(bias_b[:, :], b_b.rearrange("(a n) -> a n", a=1).to_broadcast([H, 1])).then_inc(c_in, 16)

            def load_x(k, r, c):
                sp.dma_start(xt[:, r, :, c, :], x[:, bass.ds(CG * k + c, 1), :, :].rearrange("b c h w -> h (b c) w"))\
                  .then_inc(x_in[r], 16)

            def load_band(k, p, c):
                row = diag_dram[bass.ds(CG * k + c, 1), :]
                sp.dma_start(band_raw[:, p, c, :], bass.AP(row.tensor, row.offset, [[NM, H], [1, H * NM]]))\
                  .then_inc(band_in[p], 16)

            for k in range(2):
                for c in range(CG):
                    load_x(k, k, c)
            sp.wait_ge(k_step, 12)
            sp.dma_start(diag_dram[:, :], diag[:, :, :].rearrange("k d m -> k (d m)")).then_inc(k_out, 16)
            sp.dma_start(unscale_dram[:, :], k_unscale[:, :]).then_inc(k_out, 16)
            sp.wait_ge(k_out, 32)
            for c in range(CG):
                load_band(0, 0, c)
            with nc.allow_non_contiguous_dma(reason="one value for each partition and kernel"):
                sp.dma_start(unscale[:, :], unscale_dram.rearrange("k a -> a k").to_broadcast([H, NK])).then_inc(c_in, 16)
            shared = diag_dram[C:NK, :]
            sp.dma_start(band3_raw[:, :], bass.AP(shared.tensor, shared.offset, [[NM, H], [1, H * NM]])).then_inc(c_in, 16)
            for c in range(CG):
                load_band(1, 1, c)

            for k in range(2, NX):
                for c in range(CG):
                    load_x(k, k, c)

            def slot(k, r):
                p = r % 2
                if not static(k) or k + 2 < NU:
                    for c in range(CG):
                        sp.wait_ge(flipped, CG * k + c + 1)
                        load_band(k + 2, p, c)
                if not static(k) or k + NX < NU:
                    for c in range(CG):
                        sp.wait_ge(evac1_done, CG * k + c + 1)
                        load_x(k + NX, r, c)
                if not static(k) or k > 0:
                    for c in range(CG):
                        sp.wait_ge(out_done, CG * (k - 1) + c + 1)
                        sp.dma_start(out[:, bass.ds(CG * (k - 1) + c, 1), :, :].rearrange("b c h w -> h (b c) w"),
                                     out_t[:, 1 - p, c, :].rearrange("h (b w) -> h b w", b=NB))\
                          .then_inc(stored[1 - p], 16)

            over_slots(sp, slot, NU - 5)
            for p in range(2):
                sp.wait_ge(stored[p], landed(NU - 2 + p, 2, p))

        @block.tensor
        def _(pe):
            def conv(which, k, p, c, taps):
                src_hi, src_lo, dst = gn_hi[which], gn_lo[which], (ps1, ps2)[which]
                band = band5[:, p, c, :] if which == X else band3[:, :]
                parts = [(t, m, src) for t in taps for m, src in ((t, src_hi), (t, src_lo), (K5 + t, src_hi))]
                for n, (t, m, src) in enumerate(parts):
                    mm = nc.tensor.matmul(dst[:, c, :], band[:, m::NM], src[:, p, :, c, t:t + W],
                                          start=(n == 0), stop=(n == len(parts) - 1))
                mm.then_inc(conv_done[which], 1)

            def mean_product(q):
                if q > 0 if static(q) else True:
                    pe.wait_ge(var_read, q)
                pe.wait_ge(stats_done, q + 1)
                nc.tensor.matmul(ps_s[:, 0:4 * NB], ones_mean[:, :],
                                 stats[:, :, :, :].rearrange("h s b (e t) -> h (s b) e t", e=2)[:, :, :, 1],
                                 start=True, stop=True).then_inc(mean_done, 1)

            def var_product(q):
                pe.wait_ge(dev_done, q + 1)
                nc.tensor.matmul(ps_s[:, 0:12 * NB], ones_var[:, :], stats[:, :, :, :].rearrange("h s b t -> h (s b t)"),
                                 start=True, stop=True).then_inc(var_done, 1)

            pe.wait_ge(const_ready, 3)
            mean_product(0)
            var_product(0)
            pe.wait_ge(pads_zero, 8)

            def slot(k, r):
                p = r % 2
                if not static(k) or k < NU:
                    pe.wait_ge(hi_done[X], NB * (k + 1))
                    pe.wait_ge(lo_done[X], k + 1)
                    for c in range(CG):
                        pe.wait_ge(flipped, CG * k + c + 1)
                        if not static(k) or k > 0:
                            pe.wait_ge(evac1_done, CG * (k - 1) + c + 1)
                        conv(X, k, p, c, range(K5))
                for c in range(CG):
                    if not static(k) or k > 0:
                        if c == 0:
                            if static(k) and k == 1:
                                pe.wait_ge(flip3_done, 1)
                            pe.wait_ge(hi_done[Y], NB * k)
                            pe.wait_ge(lo_done[Y], k)
                        if not static(k) or k > 1:
                            pe.wait_ge(conv_b_done, CG * (k - 2) + c + 1)
                        conv(Y, k - 1, 1 - p, c, range(1, K5 - 1))
                    if not static(k) or k < NU:
                        if c == 1:
                            mean_product(k + 1)
                        elif c == 2:
                            var_product(k + 1)

            over_slots(pe, slot, NU - 1)

        @block.scalar
        def _(act):
            act.wait_ge(const_ready, 3)

            def root(q):
                act.wait_ge(norm_step, NORM_OPS * q + 3)
                nc.scalar.activation(std[:, :], var[:, :], ACT.Sqrt, bias=eps_t[:, 0:1]).then_inc(std_done, 1)

            def normalize(s, n, r, q, at):
                act.wait_ge(affine_ready, q + 1)
                if not static(n) or n > 0:
                    act.wait_ge(lo_done[s], n)
                if not static(n) or n > 1:
                    act.wait_ge(conv_done[s], CG * (n - 1))
                for b in range(NB):
                    src = (xt, x1)[s][:, r, b, :, :]
                    by = dict(bias=g_add[:, at + b:at + b + 1], scale=g_mul[:, at + b:at + b + 1])
                    nc.scalar.activation(gn_f[s][:, b, :, :], src, ACT.Identity, **by).then_inc(gn_done[s], 1)
                    nc.scalar.activation(gn_hi[s][:, r % 2, b, :, PAD:PAD + W], src,
                                         ACT.Identity, **by).then_inc(hi_done[s], 1)

            root(0)
            normalize(X, 0, 0, 0, 0)
            act.wait_ge(c_in, 48)

            def slot(k, r):
                p = r % 2
                if not static(k) or k > 0:
                    root(k)
                    normalize(Y, k - 1, 1 - p, k, NB)
                if not static(k) or k + 1 < NU:
                    normalize(X, k + 1, (r + 1) % NX, k, NB if static(k) and k == 0 else 0)
                if not static(k) or k > 0:
                    for c in range(CG):
                        act.wait_ge(conv_done[Y], CG * (k - 1) + c + 1)
                        if not static(k) or k > 2:
                            act.wait_ge(out_done, CG * (k - 3) + c + 1)
                        nc.scalar.activation(conv_b[:, 1 - p, c, :], ps2[:, c, :], ACT.Identity, bias=bias_b[:, 0:1],
                                             scale=unscale[:, C:NK]).then_inc(conv_b_done, 1)

            over_slots(act, slot, NU - 1)

        @block.vector
        def _(dve):
            for t in (k_w1[:, :], k_w3[:, :, :], k_w5[:, :, :], k_alpha[:, :]):
                nc.vector.memset(t, 0.0).then_inc(k_zero, 1)
            dve.wait_ge(k_zero, 4)
            nc.vector.memset(k_alpha[C:NK, 2:3], 1.0).then_inc(k_zero, 1)
            nc.vector.memset(ones_mean[:, :], 1.0 / (2 * H)).then_inc(const_ready, 1)
            nc.vector.memset(ones_var[:, :], 1.0 / (2 * H * HALF)).then_inc(const_ready, 1)
            nc.vector.memset(eps_t[:, :], GN_EPS).then_inc(const_ready, 1)
            for s in (X, Y):
                for part in (gn_hi, gn_lo):
                    for at in (0, PAD + W):
                        nc.vector.memset(part[s][:, :, :, :, at:at + PAD].rearrange("h p b c w -> h (p b c) w"), 0.0)\
                          .then_inc(pads_zero, 1)

            dve.wait_ge(k_in, 80)
            nc.vector.tensor_scalar(kern[:, :, :], k_w5[:, :, :], k_alpha[:, 3:4], None, ALU.mult).then_inc(k_step, 1)
            nc.vector.scalar_tensor_tensor(out=k_mid[:, :], in0=k_w1[:, :], scalar=k_alpha[:, 1:2], in1=k_alpha[:, 0:1],
                                           op0=ALU.mult, op1=ALU.add).then_inc(k_step, 1)
            dve.wait_ge(k_step, 2)
            nc.vector.scalar_tensor_tensor(out=kern[:, 1:4, 1:4], in0=k_w3[:, :, :], scalar=k_alpha[:, 2:3],
                                           in1=kern[:, 1:4, 1:4], op0=ALU.mult, op1=ALU.add).then_inc(k_step, 1)
            dve.wait_ge(k_step, 3)
            nc.vector.tensor_tensor(kern[:, 2, 2:3], kern[:, 2, 2:3], k_mid[:, :], ALU.add).then_inc(k_step, 1)
            dve.wait_ge(k_step, 4)
            nc.vector.tensor_reduce(k_max[:, :], kern[:, :, :], AX.XY, ALU.max)
            nc.vector.tensor_reduce(k_min[:, :], kern[:, :, :], AX.XY, ALU.min).then_inc(k_step, 1)
            dve.wait_ge(k_step, 5)
            nc.vector.scalar_tensor_tensor(out=k_pow[:, :], in0=k_min[:, :], scalar=-1.0, in1=k_max[:, :],
                                           op0=ALU.mult, op1=ALU.max).then_inc(k_step, 1)
            dve.wait_ge(k_step, 6)
            nc.vector.tensor_scalar(k_pow[:, :], k_pow[:, :], 2.0 ** -100, None, ALU.max).then_inc(k_step, 1)
            dve.wait_ge(k_step, 7)
            nc.vector.tensor_scalar(k_pow[:, :].bitcast(i32), k_pow[:, :].bitcast(i32), 0x7F800000, None,
                                    ALU.bitwise_and).then_inc(k_step, 1)
            dve.wait_ge(k_step, 8)
            nc.vector.reciprocal(k_inv[:, :], k_pow[:, :])
            nc.vector.tensor_scalar(k_unscale[:, :], k_pow[:, :], 1.0 / (W_SCALE * G_SCALE), None, ALU.mult)\
              .then_inc(k_step, 1)
            dve.wait_ge(k_step, 9)
            nc.vector.tensor_scalar(kern[:, :, :], kern[:, :, :], k_inv[:, 0:1], W_SCALE, ALU.mult, ALU.mult)\
              .then_inc(k_step, 1)
            dve.wait_ge(k_step, 10)
            dve.wait_ge(diag_zero, 1)
            mid = diag[:, H - 1 - PAD:H + PAD, :]
            nc.vector.tensor_copy(mid[:, :, 0:K5], kern[:, :, :]).then_inc(k_step, 1)
            dve.wait_ge(k_step, 11)
            nc.vector.tensor_tensor(mid[:, :, K5:NM], kern[:, :, :], mid[:, :, 0:K5], ALU.subtract).then_inc(k_step, 1)

            def row_stats(at, src):
                for b in range(NB):
                    st = nc.vector.bn_stats(stats[:, at, b, :], src[:, b, :, :].rearrange("h c w -> h (c w)"))
                return st

            def deviations(q):
                halves = stats[:, :, :, :].rearrange("h s b (e t) -> h (s b) e t", e=2)[:, :, :, 1]
                dve.wait_ge(mean_done, q + 1)
                nc.vector.tensor_reduce(mean[:, :], ps_s[:, 0:4 * NB].rearrange("h (b e) -> h b e", e=2),
                                        AX.X, ALU.add).then_inc(norm_step, 1)
                dve.wait_ge(norm_step, NORM_OPS * q + 1)
                nc.vector.tensor_tensor(dev[:, :, :], halves, mean[:, :].unsqueeze(2).to_broadcast([H, 2 * NB, 2]),
                                        ALU.subtract).then_inc(norm_step, 1)
                dve.wait_ge(norm_step, NORM_OPS * q + 2)
                nc.vector.scalar_tensor_tensor(out=halves, in0=dev[:, :, :], scalar=float(HALF), in1=dev[:, :, :],
                                               op0=ALU.mult, op1=ALU.mult).then_inc(dev_done, 1)

            def affine(q):
                dve.wait_ge(var_done, q + 1)
                sums = ps_s[:, 0:12 * NB].rearrange("h (b e t) -> h b e t", e=2, t=3)[:, :, :, 1:3]
                nc.vector.tensor_reduce(var[:, :], sums, AX.XY, ALU.add).then_inc(norm_step, 1)
                dve.wait_ge(norm_step, NORM_OPS * q + 3)
                nc.vector.tensor_scalar(var_eps[:, :], var[:, :], GN_EPS, None, ALU.add).then_inc(var_read, 1)
                dve.wait_ge(std_done, q + 1)
                nc.vector.reciprocal(r0[:, :], std[:, :]).then_inc(norm_step, 1)
                dve.wait_ge(norm_step, NORM_OPS * q + 4)
                nc.vector.tensor_tensor(newton[:, :], r0[:, :], r0[:, :], ALU.mult).then_inc(norm_step, 1)
                dve.wait_ge(norm_step, NORM_OPS * q + 5)
                nc.vector.tensor_tensor(newton[:, :], newton[:, :], var_eps[:, :], ALU.mult).then_inc(norm_step, 1)
                dve.wait_ge(norm_step, NORM_OPS * q + 6)
                nc.vector.tensor_scalar(newton[:, :], newton[:, :], -0.5 * G_SCALE, 1.5 * G_SCALE,
                                        ALU.mult, ALU.add).then_inc(norm_step, 1)
                dve.wait_ge(norm_step, NORM_OPS * q + 7)
                if not static(q) or q > 0:
                    dve.wait_ge(hi_done[X], NB * (NU if static(q) and q == NU else q + 1))
                if not static(q) or q > 1:
                    dve.wait_ge(hi_done[Y], NB * (q - 1))
                nc.vector.tensor_tensor(g_mul[:, :], newton[:, :], r0[:, :], ALU.mult).then_inc(norm_step, 1)
                dve.wait_ge(norm_step, NORM_OPS * q + 8)
                nc.vector.scalar_tensor_tensor(out=g_add[:, :], in0=mean[:, :], scalar=-1.0, in1=g_mul[:, :],
                                               op0=ALU.mult, op1=ALU.mult).then_inc(affine_ready, 1)

            def low_part(s, n, p):
                dve.wait_ge(hi_done[s], NB * (n + 1))
                if not static(n) or n > 1:
                    dve.wait_ge(conv_done[s], CG * (n - 1))
                nc.vector.tensor_tensor(gn_lo[s][:, p, :, :, PAD:PAD + W].rearrange("h b c w -> h (b c) w"),
                                        gn_f[s][:, :, :, :].rearrange("h b c w -> h (b c) w"),
                                        gn_hi[s][:, p, :, :, PAD:PAD + W].rearrange("h b c w -> h (b c) w"),
                                        ALU.subtract).then_inc(lo_done[s], 1)

            def in_order(dst, src):
                return nc.vector.tensor_copy(dst.bitcast(i32).rearrange("h (o m) -> h o m", m=NM // 2),
                                             src.bitcast(i32).rearrange("h (o m) -> h o m", m=NM // 2)[:, ::-1, :])

            def in_order_unit(k, p):
                dve.wait_ge(band_in[p], landed(k, 2, p))
                for c in range(CG):
                    if not static(k) or k > 1:
                        dve.wait_ge(conv_done[X], CG * (k - 2) + c + 1)
                    in_order(band5[:, p, c, :], band_raw[:, p, c, :]).then_inc(flipped, 1)

            def evacuate(k, r, c):
                dve.wait_ge(conv_done[X], CG * k + c + 1)
                if not static(k) or k > 1:
                    dve.wait_ge(out_done, CG * (k - 2) + c + 1)
                nc.vector.scalar_tensor_tensor(
                    out=x1[:, r % 2, :, c, :], in0=ps1[:, c, :].rearrange("h (b w) -> h b w", b=NB),
                    scalar=unscale[:, bass.ds(CG * k + c, 1)], in1=xt[:, r, :, c, :],
                    op0=ALU.mult, op1=ALU.add).then_inc(evac1_done, 1)

            for k in range(2):
                dve.wait_ge(x_in[k], landed(k, NX, k))
                st = row_stats(k, xt[:, k, :, :, :])
            st.then_inc(stats_done, 1)
            deviations(0)
            affine(0)
            in_order_unit(0, 0)
            low_part(X, 0, 0)
            dve.wait_ge(c_in, 48)
            in_order(band3[:, :], band3_raw[:, :]).then_inc(flip3_done, 1)

            def slot(k, r):
                p = r % 2
                runs = not static(k) or k < NU
                if not static(k) or k > 0:
                    affine(k)
                if not static(k) or k + 2 < NU:
                    dve.wait_ge(x_in[(r + 2) % NX], landed(k + 2, NX, (r + 2) % NX))
                    dve.wait_ge(var_done, k + 1)
                    row_stats(X, xt[:, (r + 2) % NX, :, :, :])
                if runs:
                    evacuate(k, r, 0)
                if not static(k) or k + 1 < NU:
                    in_order_unit(k + 1, 1 - p)
                if not static(k) or k > 0:
                    low_part(Y, k - 1, 1 - p)
                if runs:
                    evacuate(k, r, 1)
                    evacuate(k, r, 2)
                    dve.wait_ge(evac1_done, CG * (k + 1))
                    row_stats(Y, x1[:, p, :, :, :]).then_inc(stats_done, 1)
                if not static(k) or k + 1 < NU:
                    low_part(X, k + 1, 1 - p)
                if runs:
                    deviations(k + 1)

            over_slots(dve, slot, NU - 5)

        @block.gpsimd
        def _(pool):
            nc.gpsimd.memset(diag[:, :, :], 0.0).then_inc(diag_zero, 1)

            def residual_sum(k, p):
                for c in range(CG):
                    pool.wait_ge(conv_b_done, CG * k + c + 1)
                    if c == 0 and (not static(k) or k > 1):
                        pool.wait_ge(stored[p], landed(k - 2, 2, p))
                    nc.gpsimd.tensor_tensor(out_t[:, p, c, :].rearrange("h (b w) -> h b w", b=NB), x1[:, p, :, c, :],
                                            conv_b[:, p, c, :].rearrange("h (b w) -> h b w", b=NB),
                                            ALU.add).then_inc(out_done, 1)

            residual_sum(0, 0)
            residual_sum(1, 1)
            with pool.Fori(2, NU, 2) as k:
                residual_sum(k, 0)
                residual_sum(k + 1, 1)


_INS = ["x", "L0_conv_w1", "L0_conv_w3", "L0_conv_w5", "L0_conv_alpha", "L1_conv_w", "L1_conv_b"]


def kernel(**inputs):
    import numpy as _np
    import concourse.bacc as _bacc
    from concourse import mybir as _mybir
    from concourse.bass_utils import run_bass_kernel_spmd as _run

    nc = _bacc.Bacc("TRN2", target_bir_lowering=False, num_devices=1)
    arrays, args = {}, []
    for name in _INS:
        a = _np.ascontiguousarray(inputs[name])
        arrays[f"in_{name}_dram"] = a
        args.append(nc.dram_tensor(f"in_{name}_dram", a.shape, _mybir.dt.from_np(a.dtype), kind="ExternalInput").ap())
    args.append(nc.dram_tensor("out_0_dram", inputs["x"].shape, _mybir.dt.float32, kind="ExternalOutput").ap())
    preact_conv_stack(nc, *args)
    r = _run(nc, [arrays], core_ids=[0])
    return r.results[0]["out_0_dram"]
```

```python
import concourse.bass as bass
from concourse import mybir
from contextlib import ExitStack



def preact_conv_stack(nc: bass.Bass, x: bass.AP, w1: bass.AP, w3: bass.AP, w5: bass.AP, alpha: bass.AP,
                      w_b: bass.AP, b_b: bass.AP, out: bass.AP):
    fp32 = mybir.dt.float32
    fp16 = mybir.dt.float16
    i32 = mybir.dt.int32
    ALU = mybir.AluOpType
    ACT = mybir.ActivationFunctionType
    AX = mybir.AxisListType

    NB, C, H, W = x.shape
    GROUPS = 32
    CG = C // GROUPS
    NU = GROUPS
    CH = NB * W
    NX = 4
    K5 = 5
    PAD = K5 // 2
    WP = W + 2 * PAD
    NM = 2 * K5
    TOEP = 2 * H - 1
    NK = C + 1
    GN_EPS = 1e-5
    HALF = CG * W // 2
    G_SCALE = 256.0
    W_SCALE = 2.0 ** 14

    ctx = ExitStack()
    with ctx:
        def sb(name, shape, dt=fp32):
            return ctx.enter_context(nc.sbuf_tensor(name, shape, dt))

        def sem(name):
            return ctx.enter_context(nc.semaphore(name))

        diag_dram = nc.dram_tensor("diag_scratch", [NK, TOEP * NM], fp16, kind="Internal").ap()
        unscale_dram = nc.dram_tensor("unscale_scratch", [NK, 1], fp32, kind="Internal").ap()

        k_w1 = sb("k_w1", [NK, 1])
        k_w3 = sb("k_w3", [NK, 3, 3])
        k_w5 = sb("k_w5", [NK, K5, K5])
        k_alpha = sb("k_alpha", [NK, 4])
        kern = sb("kern", [NK, K5, K5])
        k_mid = sb("k_mid", [NK, 1])
        k_max = sb("k_max", [NK, 1])
        k_min = sb("k_min", [NK, 1])
        k_pow = sb("k_pow", [NK, 1])
        k_inv = sb("k_inv", [NK, 1])
        k_unscale = sb("k_unscale", [NK, 1])
        diag = sb("diag", [NK, TOEP, NM], fp16)

        unscale = sb("unscale", [H, NK])
        bias_b = sb("bias_b", [H, 1])
        ones_mean = sb("ones_mean", [H, H])
        ones_var = sb("ones_var", [H, H])
        eps_t = sb("eps_t", [H, 1])
        warm = sb("warm", [H, 1])
        band3 = sb("band3", [H, H * NM], fp16)

        xt = sb("xt", [H, NX, NB, CG, W])
        band3_raw = sb("band3_raw", [H, H * NM], fp16)
        band_raw = sb("band_raw", [H, 2, CG, H * NM], fp16)
        band5 = sb("band5", [H, 2, CG, H * NM], fp16)
        x1 = sb("x1", [H, 2, NB, CG, W])
        gn_f = [sb(f"gn_f{s}", [H, NB, CG, W]) for s in "XY"]
        gn_hi = [sb(f"gn_hi{s}", [H, 2, NB, CG, WP], fp16) for s in "XY"]
        gn_lo = [sb(f"gn_lo{s}", [H, 2, NB, CG, WP], fp16) for s in "XY"]
        conv_b = sb("conv_b", [H, 2, CG, CH])
        out_t = sb("out_t", [H, 2, CG, CH])

        stats = sb("stats", [H, 2, NB, 6])
        mean = sb("mean", [H, 2 * NB])
        dev = sb("dev", [H, 2 * NB, 2])
        var = sb("var", [H, 2 * NB])
        var_eps = sb("var_eps", [H, 2 * NB])
        std = sb("std", [H, 2 * NB])
        r0 = sb("r0", [H, 2 * NB])
        newton = sb("newton", [H, 2 * NB])
        g_mul = sb("g_mul", [H, 2 * NB])
        g_add = sb("g_add", [H, 2 * NB])

        ps1 = ctx.enter_context(nc.psum_tensor("ps1", [H, CG, CH], fp32))
        ps2 = ctx.enter_context(nc.psum_tensor("ps2", [H, CG, CH], fp32))
        ps_s = ctx.enter_context(nc.psum_tensor("ps_s", [H, CH], fp32))

        k_in = sem("k_in")
        k_rest = sem("k_rest")
        diag_zero = sem("diag_zero")
        k_step = sem("k_step")
        k_first_out = sem("k_first_out")
        k_out = sem("k_out")
        c_in = sem("c_in")
        const_ready = sem("const_ready")
        pads_zero = sem("pads_zero")
        flipped = sem("flipped")
        flip3_done = sem("flip3_done")
        x_first_in = [[sem(f"x_first_in{k}_{b}") for b in range(NB)] for k in range(2)]
        x_in = [sem(f"x_in{r}") for r in range(NX)]
        band_in = [sem(f"band_in{p}") for p in range(2)]
        stored = [sem(f"stored{p}") for p in range(2)]
        conv_done = [sem("conv1_done"), sem("conv2_done")]
        evac1_done = sem("evac1_done")
        stats_done = sem("stats_done")
        mean_done = sem("mean_done")
        dev_done = sem("dev_done")
        var_done = sem("var_done")
        var_read = sem("var_read")
        std_done = sem("std_done")
        norm_step = sem("norm_step")
        affine_ready = sem("affine_ready")
        gn_done = [sem(f"gn_done{s}") for s in "XY"]
        hi_done = [sem(f"hi_done{s}") for s in "XY"]
        lo_done = [sem(f"lo_done{s}") for s in "XY"]
        conv_b_done = sem("conv_b_done")
        out_done = sem("out_done")
        last_x1b_done = sem("last_x1b_done")
        last_out_done = sem("last_out_done")
        X, Y = 0, 1
        NORM_OPS = 8
        WARM_UP = 11

        block = ctx.enter_context(nc.Block())

        LAST = NU - 1
        PEEL = 3

        def over_slots(eng, slot, end):
            for k in range(PEEL):
                slot(k, k % NX)
            with eng.Fori(PEEL, end - NX + 1, NX) as k:
                for j in range(NX):
                    slot(k + j, (PEEL + j) % NX)
            for k in range(end, NU + 1):
                slot(k, k % NX)

        def static(k):
            return isinstance(k, int)

        def landed(n, buffers, r):
            return 16 * CG // buffers * (n - r) + 16 * CG

        def x_landed(n, r):
            return landed(n, NX, r) - (16 * CG if r < 2 else 0)

        def x1_of(n, p):
            return xt[:, LAST % NX, :, :, :] if static(n) and n == LAST else x1[:, p, :, :, :]

        def load_x(eng, k, r, c):
            eng.dma_start(xt[:, r, :, c, :], x[:, bass.ds(CG * k + c, 1), :, :].rearrange("b c h w -> h (b c) w"))\
               .then_inc(x_in[r], 16)

        @block.sync
        def _(sp):
            with nc.allow_non_contiguous_dma(reason="a few small weights"):
                sp.dma_start(k_w1[0:C, :], w1.rearrange("c a h w -> c (a h w)")).then_inc(k_in, 16)
                sp.dma_start(k_w5[0:C, :, :], w5.rearrange("c a h w -> c (a h) w")).then_inc(k_in, 16)
                sp.dma_start(k_w3[C:NK, :, :], w_b.rearrange("c a h w -> c (a h) w")).then_inc(k_in, 16)
                sp.dma_start(bias_b[:, :], b_b.rearrange("(a n) -> a n", a=1).to_broadcast([H, 1])).then_inc(c_in, 16)

            def load_band(k, p, c):
                row = diag_dram[bass.ds(CG * k + c, 1), :]
                sp.dma_start(band_raw[:, p, c, :], bass.AP(row.tensor, row.offset, [[NM, H], [1, H * NM]]))\
                  .then_inc(band_in[p], 16)

            sp.wait_ge(k_step, 12)
            sp.dma_start(diag_dram[0:CG, :], diag[0:CG, :, :].rearrange("k d m -> k (d m)")).then_inc(k_first_out, 16)
            sp.dma_start(diag_dram[CG:NK, :], diag[CG:NK, :, :].rearrange("k d m -> k (d m)")).then_inc(k_out, 16)
            sp.dma_start(unscale_dram[:, :], k_unscale[:, :]).then_inc(k_out, 16)
            sp.wait_ge(k_first_out, 16)
            for c in range(CG):
                load_band(0, 0, c)
            sp.wait_ge(k_out, 32)
            with nc.allow_non_contiguous_dma(reason="one value for each partition and kernel"):
                sp.dma_start(unscale[:, :], unscale_dram.rearrange("k a -> a k").to_broadcast([H, NK])).then_inc(c_in, 16)
            shared = diag_dram[C:NK, :]
            sp.dma_start(band3_raw[:, :], bass.AP(shared.tensor, shared.offset, [[NM, H], [1, H * NM]])).then_inc(c_in, 16)
            for c in range(CG):
                load_x(sp, 2, 2, c)
            for c in range(CG):
                load_band(1, 1, c)
            for c in range(CG):
                load_x(sp, 3, 3, c)

            def slot(k, r):
                p = r % 2
                if not static(k) or k + 2 < NU:
                    for c in range(CG):
                        sp.wait_ge(flipped, CG * k + c + 1)
                        load_band(k + 2, p, c)
                if not static(k) or k + NX < NU:
                    for c in range(CG):
                        sp.wait_ge(evac1_done, CG * k + c + 1)
                        load_x(sp, k + NX, r, c)
                if not static(k) or k > 0:
                    for c in range(CG):
                        if static(k) and k == NU:
                            sp.wait_ge(last_out_done, c + 1)
                        else:
                            sp.wait_ge(out_done, CG * (k - 1) + c + 1)
                        sp.dma_start(out[:, bass.ds(CG * (k - 1) + c, 1), :, :].rearrange("b c h w -> h (b c) w"),
                                     out_t[:, 1 - p, c, :].rearrange("h (b w) -> h b w", b=NB))\
                          .then_inc(stored[1 - p], 16)

            over_slots(sp, slot, NU - 5)
            for p in range(2):
                sp.wait_ge(stored[p], landed(NU - 2 + p, 2, p))

        @block.tensor
        def _(pe):
            def conv(which, k, p, c, taps, part):
                src_hi, src_lo, dst = gn_hi[which], gn_lo[which], (ps1, ps2)[which]
                band = band5[:, p, c, :] if which == X else band3[:, :]
                parts = [(t, m, src_hi) for t in taps for m in (t, K5 + t)] + [(t, t, src_lo) for t in taps]
                for n in range(len(parts))[part]:
                    t, m, src = parts[n]
                    if c == 0 and src is src_lo and t == taps[0]:
                        pe.wait_ge(lo_done[which], k + 1)
                    mm = nc.tensor.matmul(dst[:, c, :], band[:, m::NM], src[:, p, :, c, t:t + W],
                                          start=(n == 0), stop=(n == len(parts) - 1))
                if n == len(parts) - 1:
                    mm.then_inc(conv_done[which], 1)

            def mean_product(q):
                if not static(q) or q > 0:
                    pe.wait_ge(var_read, q)
                pe.wait_ge(stats_done, q + 1)
                nc.tensor.matmul(ps_s[:, 0:4 * NB], ones_mean[:, :],
                                 stats[:, :, :, :].rearrange("h s b (e t) -> h (s b) e t", e=2)[:, :, :, 1],
                                 start=True, stop=True).then_inc(mean_done, 1)

            def var_product(q):
                pe.wait_ge(dev_done, q + 1)
                nc.tensor.matmul(ps_s[:, 0:12 * NB], ones_var[:, :], stats[:, :, :, :].rearrange("h s b t -> h (s b t)"),
                                 start=True, stop=True).then_inc(var_done, 1)

            WHOLE = slice(None)

            def first_conv(k, p, c, part=WHOLE):
                if c == 0:
                    pe.wait_ge(hi_done[X], NB * (k + 1))
                pe.wait_ge(flipped, CG * k + c + 1)
                if not static(k) or k > 0:
                    pe.wait_ge(evac1_done, CG * (k - 1) + c + 1)
                conv(X, k, p, c, range(K5), part)

            def second_conv(k, p, c, part=WHOLE):
                if c == 0:
                    if static(k) and k == 0:
                        pe.wait_ge(flip3_done, 1)
                    pe.wait_ge(hi_done[Y], NB * (k + 1))
                if not static(k) or k > 0:
                    pe.wait_ge(conv_b_done, CG * (k - 1) + c + 1)
                conv(Y, k, p, c, range(1, K5 - 1), part)

            pe.wait_ge(const_ready, 3)
            mean_product(0)
            var_product(0)
            for _ in range(WARM_UP):
                nc.tensor.matmul(ps2[:, 0, 0:H], ones_mean[:, :], ones_mean[:, :], start=True, stop=True)
            pe.wait_ge(pads_zero, 8)

            def step_within_first_conv(k, head):
                p = k % 2
                first_conv(k, p, 0, slice(0, head))
                mean_product(k)
                first_conv(k, p, 0, slice(head, None))
                first_conv(k, p, 1, slice(0, 4))
                var_product(k)
                first_conv(k, p, 1, slice(4, None))
                first_conv(k, p, 2)

            def first_slots():
                for c in range(CG):
                    first_conv(0, 0, c)
                step_within_first_conv(1, 13)
                for c in range(CG):
                    second_conv(0, 0, c)
                step_within_first_conv(2, 14)
                second_conv(1, 1, 0)
                second_conv(1, 1, 1)
                second_conv(1, 1, 2, slice(0, 6))
                mean_product(3)
                second_conv(1, 1, 2, slice(6, None))
                var_product(3)

            def last_slots():
                for c in range(CG):
                    first_conv(LAST - 1, (LAST - 1) % 2, c)
                first_conv(LAST, LAST % 2, 0)
                mean_product(LAST)
                first_conv(LAST, LAST % 2, 1)
                var_product(LAST)
                first_conv(LAST, LAST % 2, 2)
                second_conv(LAST - 2, LAST % 2, 0)
                second_conv(LAST - 2, LAST % 2, 1)
                mean_product(NU)
                second_conv(LAST - 2, LAST % 2, 2)
                var_product(NU)
                for k in (LAST - 1, LAST):
                    for c in range(CG):
                        second_conv(k, k % 2, c)

            def slot(k, r):
                p = r % 2
                if static(k) and k >= LAST - 1:
                    if k == LAST - 1:
                        last_slots()
                    return
                if static(k) and k < PEEL:
                    if k == 0:
                        first_slots()
                    return
                for c in range(CG):
                    first_conv(k, p, c)
                second_conv(k - 1, 1 - p, 0)
                second_conv(k - 1, 1 - p, 1)
                mean_product(k + 1)
                second_conv(k - 1, 1 - p, 2)
                var_product(k + 1)

            over_slots(pe, slot, NU - 5)

        @block.scalar
        def _(act):
            with nc.allow_non_contiguous_dma(reason="a few small weights"):
                act.dma_start(k_w3[0:C, :, :], w3.rearrange("c a h w -> c (a h) w")).then_inc(k_in, 16)
                act.dma_start(k_alpha[0:C, :], alpha.rearrange("(a n) -> a n", a=1).to_broadcast([C, 4])).then_inc(k_in, 16)
            for k in range(2):
                for b in range(NB):
                    act.dma_start(xt[:, k, b, :, :], x[b, CG * k:CG * (k + 1), :, :].rearrange("c h w -> h c w"))\
                       .then_inc(x_first_in[k][b], 16)
            act.wait_ge(const_ready, 3)
            nc.scalar.activation(warm[:, :], eps_t[:, :], ACT.Sqrt)

            def root(q):
                act.wait_ge(norm_step, NORM_OPS * q + 3)
                nc.scalar.activation(std[:, :], var[:, :], ACT.Sqrt, bias=eps_t[:, 0:1]).then_inc(std_done, 1)

            def normalize(s, n, r, q, at, alone=True):
                act.wait_ge(affine_ready, q + 1)
                if alone and (not static(n) or n > 0):
                    act.wait_ge(lo_done[s], n)
                if not static(n) or n > 1:
                    act.wait_ge(conv_done[s], CG * (n - 1))
                for b in range(NB):
                    src = xt[:, r, b, :, :] if s == X else x1_of(n, r)[:, b, :, :]
                    by = dict(bias=g_add[:, at + b:at + b + 1], scale=g_mul[:, at + b:at + b + 1])
                    if alone:
                        nc.scalar.activation(gn_f[s][:, b, :, :], src, ACT.Identity, **by)
                    nc.scalar.activation(gn_hi[s][:, r % 2, b, :, PAD:PAD + W], src,
                                         ACT.Identity, **by).then_inc(hi_done[s], 1)

            root(0)
            normalize(X, 0, 0, 0, 0, alone=False)
            act.wait_ge(c_in, 48)

            def evacuate(k, p, c):
                act.wait_ge(conv_done[Y], CG * k + c + 1)
                if not static(k) or k > 1:
                    act.wait_ge(out_done, CG * (k - 2) + c + 1)
                nc.scalar.activation(conv_b[:, p, c, :], ps2[:, c, :], ACT.Identity, bias=bias_b[:, 0:1],
                                     scale=unscale[:, C:NK]).then_inc(conv_b_done, 1)

            def last_slots():
                root(LAST - 1)
                normalize(X, LAST, LAST % NX, LAST - 1, 0)
                normalize(Y, LAST - 2, LAST % 2, LAST - 1, NB)
                root(LAST)
                normalize(Y, LAST - 1, (LAST - 1) % 2, LAST, NB)
                for c in range(CG):
                    evacuate(LAST - 2, LAST % 2, c)
                root(NU)
                normalize(Y, LAST, LAST % 2, NU, NB, alone=False)
                for c in range(CG):
                    evacuate(LAST - 1, (LAST - 1) % 2, c)
                    act.wait_ge(out_done, CG * (LAST - 2) + c + 1)
                    nc.scalar.activation(conv_b[:, LAST % 2, c, :].rearrange("h (b w) -> h b w", b=NB),
                                         x1_of(LAST, LAST % 2)[:, :, c, :], ACT.Identity,
                                         bias=bias_b[:, 0:1]).then_inc(last_x1b_done, 1)

            def slot(k, r):
                p = r % 2
                if static(k) and k >= LAST - 1:
                    if k == LAST - 1:
                        last_slots()
                    return
                if not static(k) or k > 0:
                    root(k)
                    normalize(Y, k - 1, 1 - p, k, NB, alone=not static(k) or k > 2)
                normalize(X, k + 1, (r + 1) % NX, k, NB if static(k) and k == 0 else 0)
                if not static(k) or k > 0:
                    for c in range(CG):
                        evacuate(k - 1, 1 - p, c)

            over_slots(act, slot, NU - 5)

        @block.vector
        def _(dve):
            for t in (k_w1[C:NK, :], k_w5[C:NK, :, :], k_alpha[C:NK, 0:2], k_alpha[C:NK, 3:4]):
                nc.vector.memset(t, 0.0).then_inc(k_rest, 1)
            nc.vector.memset(k_alpha[C:NK, 2:3], 1.0).then_inc(k_rest, 1)
            nc.vector.memset(ones_mean[:, :], 1.0 / (2 * H)).then_inc(const_ready, 1)
            nc.vector.memset(ones_var[:, :], 1.0 / (2 * H * HALF)).then_inc(const_ready, 1)
            nc.vector.memset(eps_t[:, :], GN_EPS).then_inc(const_ready, 1)
            for s in (X, Y):
                for part in (gn_hi, gn_lo):
                    for at in (0, PAD + W):
                        nc.vector.memset(part[s][:, :, :, :, at:at + PAD].rearrange("h p b c w -> h (p b c) w"), 0.0)\
                          .then_inc(pads_zero, 1)

            def row_stats(at, src):
                for b in range(NB):
                    st = nc.vector.bn_stats(stats[:, at, b, :], src[:, b, :, :].rearrange("h c w -> h (c w)"))
                return st

            def deviations(q):
                halves = stats[:, :, :, :].rearrange("h s b (e t) -> h (s b) e t", e=2)[:, :, :, 1]
                dve.wait_ge(mean_done, q + 1)
                nc.vector.tensor_reduce(mean[:, :], ps_s[:, 0:4 * NB].rearrange("h (b e) -> h b e", e=2),
                                        AX.X, ALU.add).then_inc(norm_step, 1)
                dve.wait_ge(norm_step, NORM_OPS * q + 1)
                nc.vector.tensor_tensor(dev[:, :, :], halves, mean[:, :].unsqueeze(2).to_broadcast([H, 2 * NB, 2]),
                                        ALU.subtract).then_inc(norm_step, 1)
                dve.wait_ge(norm_step, NORM_OPS * q + 2)
                nc.vector.scalar_tensor_tensor(out=halves, in0=dev[:, :, :], scalar=float(HALF), in1=dev[:, :, :],
                                               op0=ALU.mult, op1=ALU.mult).then_inc(dev_done, 1)

            def affine(q):
                dve.wait_ge(var_done, q + 1)
                sums = ps_s[:, 0:12 * NB].rearrange("h (b e t) -> h b e t", e=2, t=3)[:, :, :, 1:3]
                nc.vector.tensor_reduce(var[:, :], sums, AX.XY, ALU.add).then_inc(norm_step, 1)
                dve.wait_ge(norm_step, NORM_OPS * q + 3)
                nc.vector.tensor_scalar(var_eps[:, :], var[:, :], GN_EPS, None, ALU.add).then_inc(var_read, 1)
                dve.wait_ge(std_done, q + 1)
                nc.vector.reciprocal(r0[:, :], std[:, :]).then_inc(norm_step, 1)
                dve.wait_ge(norm_step, NORM_OPS * q + 4)
                nc.vector.tensor_tensor(newton[:, :], r0[:, :], r0[:, :], ALU.mult).then_inc(norm_step, 1)
                dve.wait_ge(norm_step, NORM_OPS * q + 5)
                nc.vector.tensor_tensor(newton[:, :], newton[:, :], var_eps[:, :], ALU.mult).then_inc(norm_step, 1)
                dve.wait_ge(norm_step, NORM_OPS * q + 6)
                nc.vector.tensor_scalar(newton[:, :], newton[:, :], -0.5 * G_SCALE, 1.5 * G_SCALE,
                                        ALU.mult, ALU.add).then_inc(norm_step, 1)
                dve.wait_ge(norm_step, NORM_OPS * q + 7)
                if not static(q) or q > 0:
                    dve.wait_ge(hi_done[X], NB * (min(q + 1, NU) if static(q) else q + 1))
                if not static(q) or q > 1:
                    dve.wait_ge(hi_done[Y], NB * (q - 1))
                nc.vector.tensor_tensor(g_mul[:, :], newton[:, :], r0[:, :], ALU.mult).then_inc(norm_step, 1)
                dve.wait_ge(norm_step, NORM_OPS * q + 8)
                nc.vector.scalar_tensor_tensor(out=g_add[:, :], in0=mean[:, :], scalar=-1.0, in1=g_mul[:, :],
                                               op0=ALU.mult, op1=ALU.mult).then_inc(affine_ready, 1)

            def low_part(s, n, p):
                dve.wait_ge(hi_done[s], NB * (n + 1))
                if not static(n) or n > 1:
                    dve.wait_ge(conv_done[s], CG * (n - 1))
                nc.vector.tensor_tensor(gn_lo[s][:, p, :, :, PAD:PAD + W].rearrange("h b c w -> h (b c) w"),
                                        gn_f[s][:, :, :, :].rearrange("h b c w -> h (b c) w"),
                                        gn_hi[s][:, p, :, :, PAD:PAD + W].rearrange("h b c w -> h (b c) w"),
                                        ALU.subtract).then_inc(lo_done[s], 1)

            def gn_batches(s, n, q, at):
                dve.wait_ge(affine_ready, q + 1)
                src = xt[:, n % NX, :, :, :] if s == X else x1_of(n, n % 2)
                for b in range(NB):
                    nc.vector.tensor_scalar(gn_f[s][:, b, :, :], src[:, b, :, :], g_mul[:, at + b:at + b + 1],
                                            g_add[:, at + b:at + b + 1], ALU.mult, ALU.add).then_inc(gn_done[s], 1)

            def low_batches(s, n, turn):
                for b in range(NB):
                    dve.wait_ge(gn_done[s], NB * turn + b + 1)
                    dve.wait_ge(hi_done[s], NB * n + b + 1)
                    lo = nc.vector.tensor_tensor(gn_lo[s][:, n % 2, b, :, PAD:PAD + W], gn_f[s][:, b, :, :],
                                                 gn_hi[s][:, n % 2, b, :, PAD:PAD + W], ALU.subtract)
                lo.then_inc(lo_done[s], 1)

            def in_order(dst, src):
                return nc.vector.tensor_copy(dst.bitcast(i32).rearrange("h (o m) -> h o m", m=NM // 2),
                                             src.bitcast(i32).rearrange("h (o m) -> h o m", m=NM // 2)[:, ::-1, :])

            def in_order_unit(k, p):
                dve.wait_ge(band_in[p], landed(k, 2, p))
                for c in range(CG):
                    if not static(k) or k > 1:
                        dve.wait_ge(conv_done[X], CG * (k - 2) + c + 1)
                    in_order(band5[:, p, c, :], band_raw[:, p, c, :]).then_inc(flipped, 1)

            def evacuate(k, r, c):
                dve.wait_ge(conv_done[X], CG * k + c + 1)
                if not static(k) or 1 < k < LAST:
                    dve.wait_ge(out_done, CG * (k - 2) + c + 1)
                nc.vector.scalar_tensor_tensor(
                    out=x1_of(k, r % 2)[:, :, c, :], in0=ps1[:, c, :].rearrange("h (b w) -> h b w", b=NB),
                    scalar=unscale[:, bass.ds(CG * k + c, 1)], in1=xt[:, r, :, c, :],
                    op0=ALU.mult, op1=ALU.add).then_inc(evac1_done, 1)

            def first_stats(k, b):
                dve.wait_ge(x_first_in[k][b], 16)
                return nc.vector.bn_stats(stats[:, k, b, :], xt[:, k, b, :, :].rearrange("h c w -> h (c w)"))

            dve.wait_ge(k_in, 80)
            dve.wait_ge(k_rest, 5)
            nc.vector.tensor_scalar(kern[:, :, :], k_w5[:, :, :], k_alpha[:, 3:4], None, ALU.mult).then_inc(k_step, 1)
            nc.vector.scalar_tensor_tensor(out=k_mid[:, :], in0=k_w1[:, :], scalar=k_alpha[:, 1:2], in1=k_alpha[:, 0:1],
                                           op0=ALU.mult, op1=ALU.add).then_inc(k_step, 1)
            dve.wait_ge(k_step, 2)
            nc.vector.scalar_tensor_tensor(out=kern[:, 1:4, 1:4], in0=k_w3[:, :, :], scalar=k_alpha[:, 2:3],
                                           in1=kern[:, 1:4, 1:4], op0=ALU.mult, op1=ALU.add).then_inc(k_step, 1)
            dve.wait_ge(k_step, 3)
            nc.vector.tensor_tensor(kern[:, 2, 2:3], kern[:, 2, 2:3], k_mid[:, :], ALU.add).then_inc(k_step, 1)
            dve.wait_ge(k_step, 4)
            nc.vector.tensor_reduce(k_max[:, :], kern[:, :, :], AX.XY, ALU.max)
            nc.vector.tensor_reduce(k_min[:, :], kern[:, :, :], AX.XY, ALU.min).then_inc(k_step, 1)
            dve.wait_ge(k_step, 5)
            nc.vector.scalar_tensor_tensor(out=k_pow[:, :], in0=k_min[:, :], scalar=-1.0, in1=k_max[:, :],
                                           op0=ALU.mult, op1=ALU.max).then_inc(k_step, 1)
            dve.wait_ge(k_step, 6)
            nc.vector.tensor_scalar(k_pow[:, :], k_pow[:, :], 2.0 ** -100, None, ALU.max).then_inc(k_step, 1)
            dve.wait_ge(k_step, 7)
            nc.vector.tensor_scalar(k_pow[:, :].bitcast(i32), k_pow[:, :].bitcast(i32), 0x7F800000, None,
                                    ALU.bitwise_and).then_inc(k_step, 1)
            dve.wait_ge(k_step, 8)
            nc.vector.reciprocal(k_inv[:, :], k_pow[:, :])
            nc.vector.tensor_scalar(k_unscale[:, :], k_pow[:, :], 1.0 / (W_SCALE * G_SCALE), None, ALU.mult)\
              .then_inc(k_step, 1)
            dve.wait_ge(k_step, 9)
            nc.vector.tensor_scalar(kern[:, :, :], kern[:, :, :], k_inv[:, 0:1], W_SCALE, ALU.mult, ALU.mult)\
              .then_inc(k_step, 1)
            first_stats(0, 0)
            dve.wait_ge(k_step, 10)
            dve.wait_ge(diag_zero, 1)
            mid = diag[:, H - 1 - PAD:H + PAD, :]
            nc.vector.tensor_copy(mid[:, :, 0:K5], kern[:, :, :]).then_inc(k_step, 1)
            first_stats(0, 1)
            dve.wait_ge(k_step, 11)
            nc.vector.tensor_tensor(mid[:, :, K5:NM], kern[:, :, :], mid[:, :, 0:K5], ALU.subtract).then_inc(k_step, 1)

            for k, b in ((0, 2), (0, 3), (1, 0), (1, 1), (1, 2), (1, 3)):
                st = first_stats(k, b)
            st.then_inc(stats_done, 1)
            deviations(0)
            affine(0)
            gn_batches(X, 0, 0, 0)
            in_order_unit(0, 0)
            low_batches(X, 0, 0)
            dve.wait_ge(c_in, 48)
            in_order(band3[:, :], band3_raw[:, :]).then_inc(flip3_done, 1)

            def x_stats(k, r):
                dve.wait_ge(x_in[r], x_landed(k, r))
                dve.wait_ge(var_done, k - 1)
                row_stats(X, xt[:, r, :, :, :])

            def x1_stats(k, p):
                dve.wait_ge(evac1_done, CG * (k + 1))
                row_stats(Y, x1_of(k, p)).then_inc(stats_done, 1)

            def first_slots():
                x_stats(2, 2)
                evacuate(0, 0, 0)
                in_order_unit(1, 1)
                evacuate(0, 0, 1)
                low_part(X, 1, 1)
                evacuate(0, 0, 2)
                x1_stats(0, 0)
                deviations(1)
                evacuate(1, 1, 0)
                affine(1)
                gn_batches(Y, 0, 1, NB)
                evacuate(1, 1, 1)
                low_batches(Y, 0, 0)
                evacuate(1, 1, 2)
                in_order_unit(2, 0)
                x_stats(3, 3)
                low_part(X, 2, 0)
                x1_stats(1, 1)
                in_order_unit(3, 1)
                deviations(2)
                evacuate(2, 2, 0)
                affine(2)
                gn_batches(Y, 1, 2, NB)
                evacuate(2, 2, 1)
                low_batches(Y, 1, 1)
                evacuate(2, 2, 2)
                x_stats(4, 0)
                x1_stats(2, 0)
                deviations(3)
                low_part(X, 3, 1)

            def last_slots():
                affine(LAST - 1)
                evacuate(LAST - 1, (LAST - 1) % NX, 0)
                in_order_unit(LAST, LAST % 2)
                evacuate(LAST - 1, (LAST - 1) % NX, 1)
                low_part(X, LAST, LAST % 2)
                evacuate(LAST - 1, (LAST - 1) % NX, 2)
                x1_stats(LAST - 1, (LAST - 1) % 2)
                deviations(LAST)
                low_part(Y, LAST - 2, LAST % 2)
                evacuate(LAST, LAST % NX, 0)
                affine(LAST)
                evacuate(LAST, LAST % NX, 1)
                evacuate(LAST, LAST % NX, 2)
                x1_stats(LAST, LAST % 2)
                deviations(NU)
                low_part(Y, LAST - 1, (LAST - 1) % 2)
                affine(NU)
                gn_batches(Y, LAST, NU, NB)
                low_batches(Y, LAST, 2)
                for c in range(CG):
                    dve.wait_ge(conv_done[Y], CG * LAST + c + 1)
                    dve.wait_ge(last_x1b_done, c + 1)
                    if c == 0:
                        dve.wait_ge(stored[LAST % 2], landed(LAST - 2, 2, LAST % 2))
                    nc.vector.scalar_tensor_tensor(out=out_t[:, LAST % 2, c, :], in0=ps2[:, c, :],
                                                   scalar=unscale[:, C:NK], in1=conv_b[:, LAST % 2, c, :],
                                                   op0=ALU.mult, op1=ALU.add).then_inc(last_out_done, 1)

            def slot(k, r):
                p = r % 2
                if static(k) and k < PEEL:
                    if k == 0:
                        first_slots()
                    return
                if static(k) and k >= LAST - 1:
                    if k == LAST - 1:
                        last_slots()
                    return
                affine(k)
                x_stats(k + 2, (r + 2) % NX)
                evacuate(k, r, 0)
                in_order_unit(k + 1, 1 - p)
                low_part(Y, k - 1, 1 - p)
                evacuate(k, r, 1)
                evacuate(k, r, 2)
                x1_stats(k, p)
                low_part(X, k + 1, 1 - p)
                deviations(k + 1)

            over_slots(dve, slot, NU - 5)

        @block.gpsimd
        def _(pool):
            nc.gpsimd.memset(diag[:, :, :], 0.0).then_inc(diag_zero, 1)

            def residual_sum(k, p):
                for c in range(CG):
                    pool.wait_ge(conv_b_done, CG * k + c + 1)
                    if c == 0 and (not static(k) or k > 1):
                        pool.wait_ge(stored[p], landed(k - 2, 2, p))
                    nc.gpsimd.tensor_tensor(out_t[:, p, c, :].rearrange("h (b w) -> h b w", b=NB), x1[:, p, :, c, :],
                                            conv_b[:, p, c, :].rearrange("h (b w) -> h b w", b=NB),
                                            ALU.add).then_inc(out_done, 1)

            residual_sum(0, 0)
            residual_sum(1, 1)
            with pool.Fori(2, LAST - 1, 2) as k:
                residual_sum(k, 0)
                residual_sum(k + 1, 1)
            residual_sum(LAST - 1, 0)


_INS = ["x", "L0_conv_w1", "L0_conv_w3", "L0_conv_w5", "L0_conv_alpha", "L1_conv_w", "L1_conv_b"]


def kernel(**inputs):
    import numpy as _np
    import concourse.bacc as _bacc
    from concourse import mybir as _mybir
    from concourse.bass_utils import run_bass_kernel_spmd as _run

    nc = _bacc.Bacc("TRN2", target_bir_lowering=False, num_devices=1)
    arrays, args = {}, []
    for name in _INS:
        a = _np.ascontiguousarray(inputs[name])
        arrays[f"in_{name}_dram"] = a
        args.append(nc.dram_tensor(f"in_{name}_dram", a.shape, _mybir.dt.from_np(a.dtype), kind="ExternalInput").ap())
    args.append(nc.dram_tensor("out_0_dram", inputs["x"].shape, _mybir.dt.float32, kind="ExternalOutput").ap())
    preact_conv_stack(nc, *args)
    r = _run(nc, [arrays], core_ids=[0])
    return r.results[0]["out_0_dram"]
```
